# Optimizing a Trainium2 kernel written in Bass

```python
import numpy as np
import jax
import jax.numpy as jnp

def _softmax(x, axis=-1):
    return jax.nn.softmax(x, axis=axis)

def _gelu(x):
    return jax.nn.gelu(x, approximate=True)

def _silu(x):
    return jax.nn.silu(x)

def _sigmoid(x):
    return jax.nn.sigmoid(x)

def _layernorm(x, axis=-1, eps=1e-05):
    m = jnp.mean(x, axis=axis, keepdims=True)
    v = jnp.var(x, axis=axis, keepdims=True)
    return (x - m) / jnp.sqrt(v + eps)

def _scatter_add(tgt, idx, src, axis=0):
    return tgt.at[idx].add(src)

def _segment_sum(src, seg, n):
    return jax.ops.segment_sum(src, seg, n)
kernel_name = 'mk_adj_preln_d1_adj_r2_5dbf74'

def setup_inputs(seed: int=0):
    np.random.seed(seed)
    _w = jnp.asarray

    def _rec_inputs():
        import jax
        import jax.numpy as jnp
        _gk = jax.random.key(seed)
        x = 7.22e-05 + 1 * jax.random.normal(jax.random.fold_in(_gk, 1), (32, 256, 256), jnp.float32)
        _a = jax.random.bernoulli(jax.random.fold_in(_gk, 2), 0.0625, (256, 256))
        _a = jnp.logical_or(_a, jnp.swapaxes(_a, -1, -2))
        _a = jnp.logical_or(_a, jnp.eye(256, dtype=bool))
        _af = _a.astype(jnp.float32)
        _af = _af * jax.random.uniform(jax.random.fold_in(_gk, 3), (256, 256), jnp.float32, 0.05, 0.00390622)
        adj = _af
        return (x, adj)
    x, adj = _rec_inputs()

    def _L0_gnn_setup():
        import jax, jax.numpy as jnp
        import numpy as np
        B, N, D, T = (64, 128, 256, 3)

        def _lin(v, W, b):
            return jnp.einsum('...i,oi->...o', v, W) + b
        key = jax.random.key(seed)
        ks = jax.random.split(key, 12)
        s2 = 1.0 / np.sqrt(2 * D)
        s1 = 1.0 / np.sqrt(D)
        return {'x': jax.random.normal(ks[0], (B, N, D), jnp.float32), 'in_mat': jax.random.uniform(ks[1], (N, N), jnp.float32) / N, 'out_mat': jax.random.uniform(ks[2], (N, N), jnp.float32) / N, 'w3_w': jax.random.normal(ks[3], (D, 2 * D), jnp.float32) * s2, 'w3_b': jnp.zeros((D,), jnp.float32), 'u3_w': jax.random.normal(ks[4], (D, D), jnp.float32) * s1, 'u3_b': jnp.zeros((D,), jnp.float32), 'w4_w': jax.random.normal(ks[5], (D, 2 * D), jnp.float32) * s2, 'w4_b': jnp.zeros((D,), jnp.float32), 'w5_w': jax.random.normal(ks[6], (D, 2 * D), jnp.float32) * s2, 'w5_b': jnp.zeros((D,), jnp.float32), 'u5_w': jax.random.normal(ks[7], (D, D), jnp.float32) * s1, 'u5_b': jnp.zeros((D,), jnp.float32)}
    _L0_gnn_all = _L0_gnn_setup()
    _L0_gnn_in = {k: v for k, v in _L0_gnn_all.items() if k in ('w3_w', 'w3_b', 'u3_w', 'u3_b', 'w4_w', 'w4_b', 'w5_w', 'w5_b', 'u5_w', 'u5_b')}
    del _L0_gnn_all
    return {'x': x, 'adj': adj, 'L0_gnn_w3_w': _L0_gnn_in['w3_w'], 'L0_gnn_w3_b': _L0_gnn_in['w3_b'], 'L0_gnn_u3_w': _L0_gnn_in['u3_w'], 'L0_gnn_u3_b': _L0_gnn_in['u3_b'], 'L0_gnn_w4_w': _L0_gnn_in['w4_w'], 'L0_gnn_w4_b': _L0_gnn_in['w4_b'], 'L0_gnn_w5_w': _L0_gnn_in['w5_w'], 'L0_gnn_w5_b': _L0_gnn_in['w5_b'], 'L0_gnn_u5_w': _L0_gnn_in['u5_w'], 'L0_gnn_u5_b': _L0_gnn_in['u5_b']}

def reference(x, adj, L0_gnn_w3_w, L0_gnn_w3_b, L0_gnn_u3_w, L0_gnn_u3_b, L0_gnn_w4_w, L0_gnn_w4_b, L0_gnn_w5_w, L0_gnn_w5_b, L0_gnn_u5_w, L0_gnn_u5_b):
    import jax
    import jax.numpy as jnp

    def _L0_gnn_ref(x, in_mat, out_mat, w3_w, w3_b, u3_w, u3_b, w4_w, w4_b, w5_w, w5_b, u5_w, u5_b):
        import jax, jax.numpy as jnp
        import numpy as np
        B, N, D, T = (64, 128, 256, 3)

        def _lin(v, W, b):
            return jnp.einsum('...i,oi->...o', v, W) + b
        h = x
        for _ in range(T):
            a_in = jnp.einsum('nm,bmd->bnd', in_mat, h)
            a_out = jnp.einsum('nm,bmd->bnd', out_mat, h)
            av = jnp.concatenate([a_in, a_out], axis=-1)
            z = jax.nn.sigmoid(_lin(av, w3_w, w3_b) + _lin(h, u3_w, u3_b))
            r = jax.nn.sigmoid(_lin(av, w4_w, w4_b) + _lin(h, u3_w, u3_b))
            hv = jnp.tanh(_lin(av, w5_w, w5_b) + _lin(r * h, u5_w, u5_b))
            h = (1.0 - z) * h + z * hv
        return h
    h = jnp.maximum(_layernorm(x, axis=-1), 0.0)
    x = x + _L0_gnn_ref(h, adj, adj, L0_gnn_w3_w, L0_gnn_w3_b, L0_gnn_u3_w, L0_gnn_u3_b, L0_gnn_w4_w, L0_gnn_w4_b, L0_gnn_w5_w, L0_gnn_w5_b, L0_gnn_u5_w, L0_gnn_u5_b)
    return x

_drawn_inputs = setup_inputs


def setup_inputs(seed=0):
    import zlib

    import numpy as np

    out = dict(_drawn_inputs(seed))
    spreads = {'L0_gnn_w3_b': (0.0, 0.417),
     'L0_gnn_u3_b': (0.0, 0.345),
     'L0_gnn_w4_b': (0.0, 0.8),
     'L0_gnn_w5_b': (0.0, 0.1),
     'L0_gnn_u5_b': (0.0, 0.1)}
    factors = {}
    for name, (base, spread) in spreads.items():
        noise = np.random.default_rng([zlib.crc32(name.encode()), seed]).standard_normal(out[name].shape)
        drawn = base * np.exp(spread * noise) if base else spread * noise
        out[name] = jnp.asarray(drawn.astype(out[name].dtype))
    for name, factor in factors.items():
        out[name] = (out[name] * factor).astype(out[name].dtype)
    return out
```

```python
from contextlib import ExitStack

import concourse.bass as bass
from concourse import mybir

F32 = mybir.dt.float32
F32R = mybir.dt.float32r
ALU = mybir.AluOpType
ACT = mybir.ActivationFunctionType

P = 128
EPS = 1e-5
STEPS = 3
STREAMS = 2


def gated_graph_network(nc, x, adj, w3_w, w3_b, u3_w, u3_b, w4_w, w4_b, w5_w, w5_b, u5_w, u5_b, out):
    B, N, D = x.shape
    KC = D // P
    NC = N // P
    GB = 2
    COLS = GB * N
    RC = GB * NC
    GROUPS = B // GB
    ROUNDS = GROUPS // STREAMS
    TPR = STEPS * STREAMS
    assert KC == 2 and NC == 2 and COLS == 512 and GROUPS % STREAMS == 0 and STREAMS == 2

    x_groups = x.rearrange("(g b) (c p) d -> g p b c d", b=GB, p=P)
    out_groups = out.rearrange("(g b) (c p) d -> g p b c d", b=GB, p=P)

    with ExitStack() as ctx:
        def sb(name, shape, dt=F32):
            return ctx.enter_context(nc.sbuf_tensor(name, shape, dt))

        def sem(name):
            return ctx.enter_context(nc.semaphore(name))

        def per_stream(name, shape, dt=F32):
            return [sb(f"{name}{s}", shape, dt) for s in range(STREAMS)]

        MATS = ("adj", "u3", "w3", "w4", "w5", "u5")
        sources = {"adj": adj, "u3": u3_w, "w3": w3_w, "w4": w4_w, "w5": w5_w, "u5": u5_w}
        folded = ("w3", "w4", "w5")
        rows = {m: sb(f"rows_{m}", [P, 2, sources[m].shape[1]]) for m in MATS}
        hi = {m: sb(f"{m}_hi", [P, 2, 256], F32R) for m in MATS}
        lo = {m: sb(f"{m}_lo", [P, 2, 256], F32R) for m in MATS}
        identity = sb("identity", [P, P])
        bias_rows = sb("bias_rows", [P, P])
        bias_cols = sb("bias_cols", [P, 10])
        gate_bias = sb("gate_bias", [P, 3, KC])
        eps_tile = sb("eps_tile", [P, RC])
        minus_half = sb("minus_half", [P, RC])
        minus_one = sb("minus_one", [P, RC])

        x_in = per_stream("x_in", [P, RC, D])
        x_kept_rows = per_stream("x_kept_rows", [P, RC, D])
        out_rows = per_stream("out_rows", [P, RC, D])
        stats = per_stream("stats", [P, RC, 6])
        mean_var = per_stream("mean_var", [P, RC, 2])
        var_eps = per_stream("var_eps", [P, RC])
        inv_std = per_stream("inv_std", [P, RC])
        mean_scaled = per_stream("mean_scaled", [P, RC])
        shift = per_stream("shift", [P, RC])
        h0_rows = per_stream("h0_rows", [P, RC, D])
        nat_hi = per_stream("nat_hi", [P, RC, D], F32R)
        nat_lo = per_stream("nat_lo", [P, RC, D], F32R)
        h0_t = per_stream("h0_t", [P, KC, COLS])
        h_t = per_stream("h_t", [P, KC, COLS])
        state_hi = per_stream("state_hi", [P, KC, COLS], F32R)
        state_lo = per_stream("state_lo", [P, KC, COLS], F32R)
        shared = per_stream("shared", [P, KC, COLS])
        z_gate = per_stream("z_gate", [P, KC, COLS])
        agg_hi = sb("agg_hi", [P, KC, COLS], F32R)
        agg_lo = sb("agg_lo", [P, KC, COLS], F32R)
        r_pre = sb("r_pre", [P, KC, COLS])
        r_gate = sb("r_gate", [P, KC, COLS])
        rh = sb("rh", [P, KC, COLS])
        rh_hi = sb("rh_hi", [P, KC, COLS], F32R)
        rh_lo = sb("rh_lo", [P, KC, COLS], F32R)
        cand = sb("cand", [P, KC, COLS])
        change = sb("change", [P, KC, COLS])
        gated_change = sb("gated_change", [P, KC, COLS])

        def bank_pair(name):
            return [ctx.enter_context(nc.psum_tensor(f"{name}{c}", [P, 512], F32)) for c in range(2)]

        agg_ps = bank_pair("agg_ps")
        z_ps = bank_pair("z_ps")
        r_ps = bank_pair("r_ps")
        cand_ps = bank_pair("cand_ps")

        mat_loaded = {m: sem(f"{m}_loaded") for m in MATS}
        bias_loaded = sem("bias_loaded")
        x_loaded = [sem(f"x_loaded{s}") for s in range(STREAMS)]
        out_rows_free = [sem(f"out_rows_free{s}") for s in range(STREAMS)]
        consts_set = sem("consts_set")
        bias_rows_zero = sem("bias_rows_zero")
        identity_set = sem("identity_set")
        folded_sum = sem("folded_sum")
        mat_turned = sem("mat_turned")
        mat_hi_set = sem("mat_hi_set")
        mat_lo_set = sem("mat_lo_set")
        bias_turned = sem("bias_turned")
        bias_copied = sem("bias_copied")
        bias_set = sem("bias_set")
        stats_done = sem("stats_done")
        mean_var_done = sem("mean_var_done")
        ln_chain = sem("ln_chain")
        ln_scale_done = sem("ln_scale_done")
        h0_done = sem("h0_done")
        h0_turned = sem("h0_turned")
        h0_t_saved = sem("h0_t_saved")
        x_kept = [sem(f"x_kept{s}") for s in range(STREAMS)]
        out_done = sem("out_done")
        shared_mm = sem("shared_mm")
        agg_mm = sem("agg_mm")
        z_mm = sem("z_mm")
        r_mm = sem("r_mm")
        cand_mm = sem("cand_mm")
        turned_mm = sem("turned_mm")
        shared_saved = sem("shared_saved")
        agg_hi_done = sem("agg_hi_done")
        agg_lo_done = sem("agg_lo_done")
        z_done = sem("z_done")
        r_pre_done = sem("r_pre_done")
        r_done = sem("r_done")
        rh_done = sem("rh_done")
        rh_hi_done = sem("rh_hi_done")
        rh_lo_done = sem("rh_lo_done")
        cand_done = sem("cand_done")
        change_done = sem("change_done")
        gated_done = sem("gated_done")
        h_done = sem("h_done")
        state_hi_done = sem("state_hi_done")
        state_lo_done = sem("state_lo_done")
        nat_hi_done = sem("nat_hi_done")
        nat_lo_done = sem("nat_lo_done")

        def count(q, c):
            return 2 * q + (c + 1)

        def run_slots(eng, slot):
            slot(0, 0, 0, True, True)
            with eng.Fori(0, ROUNDS - 1) as i:
                for j in range(1, TPR + 1):
                    slot(TPR * i + j, j, i, False, True)
            for j in range(1, TPR):
                slot(TPR * (ROUNDS - 1) + j, j, ROUNDS - 1, False, False)

        LAST = TPR * ROUNDS - 1

        def place(j):
            return j % STREAMS, (j // STREAMS) % STEPS

        def prep_bank(n, c):
            return (z_ps, r_ps, cand_ps)[n % 3][c][:, 0:256]

        block = ctx.enter_context(nc.Block())

        @block.sync
        def _(sp):
            def load_x(g, s):
                sp.dma_start(x_in[s][:].rearrange("p (b c) d -> p b c d", b=GB),
                             x_groups[g]).then_inc(x_loaded[s], 16)

            def load_mat(m):
                sp.dma_start(rows[m][:], sources[m].rearrange("(c p) k -> p c k", p=P)).then_inc(mat_loaded[m], 16)

            for s in range(STREAMS):
                sp.sem_inc(out_rows_free[s], 16)
            load_x(0, 0)
            load_mat("u3")
            load_x(1, 1)
            load_mat("w4")
            load_mat("w5")
            sp.wait_ge(bias_rows_zero, 1)
            for n, b in enumerate((w3_b, u3_b, w4_b, w5_b, u5_b)):
                sp.dma_start(bias_rows[KC * n:KC * (n + 1), :], b.rearrange("(c p) -> c p", p=P)
                             ).then_inc(bias_loaded, 16)

            def keep_x(s, i):
                sp.wait_ge(x_loaded[s], 16 * i + 16)
                sp.dma_start(x_kept_rows[s][:], x_in[s][:]).then_inc(x_kept[s], 16)

            def refill(g, s, i):
                sp.wait_ge(mean_var_done, g - 1)
                sp.wait_ge(h0_done, g - 1)
                sp.wait_ge(x_kept[s], 16 * i)
                load_x(g, s)

            def store(g, s):
                sp.wait_ge(out_done, 2 * g + 2)
                sp.dma_start(out_groups[g], out_rows[s][:].rearrange("p (b c) d -> p b c d", b=GB)
                             ).then_inc(out_rows_free[s], 16)

            for s in range(STREAMS):
                keep_x(s, 0)
                refill(STREAMS + s, s, 1)
            with sp.Fori(0, ROUNDS - 2) as i:
                for s in range(STREAMS):
                    store(STREAMS * i + s, s)
                    keep_x(s, i + 1)
                    refill(STREAMS * i + (2 * STREAMS + s), s, i + 2)
            for s in range(STREAMS):
                store(STREAMS * (ROUNDS - 2) + s, s)
                keep_x(s, ROUNDS - 1)
            for s in range(STREAMS):
                store(STREAMS * (ROUNDS - 1) + s, s)
            for s in range(STREAMS):
                sp.wait_ge(out_rows_free[s], 16 * ROUNDS + 16)

        @block.gpsimd
        def _(pool):
            nc.gpsimd.memset(identity[:], 0.0).then_inc(consts_set, 1)
            nc.gpsimd.memset(eps_tile[:], EPS).then_inc(consts_set, 1)
            nc.gpsimd.memset(minus_half[:], -0.5).then_inc(consts_set, 1)
            nc.gpsimd.memset(minus_one[:], -1.0).then_inc(consts_set, 1)
            pool.wait_ge(consts_set, 4)
            nc.gpsimd.affine_select(out=identity[:], in_=identity[:], compare_op=ALU.not_equal, fill=1.0,
                                    base=0, pattern=[[-1, P]], channel_multiplier=1).then_inc(identity_set, 1)

            def ln_scale(u, s):
                pool.wait_ge(mean_var_done, u + 1)
                nc.gpsimd.tensor_tensor(var_eps[s][:], mean_var[s][:, :, 1], eps_tile[:], ALU.add).then_inc(ln_chain, 1)
                pool.wait_ge(ln_chain, 3 * u + 1)
                nc.gpsimd.tensor_tensor(inv_std[s][:], var_eps[s][:], minus_half[:], ALU.pow).then_inc(ln_chain, 1)
                pool.wait_ge(ln_chain, 3 * u + 2)
                nc.gpsimd.tensor_tensor(mean_scaled[s][:], mean_var[s][:, :, 0], inv_std[s][:],
                                        ALU.mult).then_inc(ln_chain, 1)
                pool.wait_ge(ln_chain, 3 * u + 3)
                nc.gpsimd.tensor_tensor(shift[s][:], mean_scaled[s][:], minus_one[:],
                                        ALU.mult).then_inc(ln_scale_done, 1)

            for s in range(STREAMS):
                ln_scale(s, s)
            with pool.Fori(1, ROUNDS) as i:
                for s in range(STREAMS):
                    ln_scale(STREAMS * i + s, s)

        @block.scalar
        def _(act):
            def load_mat(m):
                act.dma_start(rows[m][:], sources[m].rearrange("(c p) k -> p c k", p=P)).then_inc(mat_loaded[m], 16)

            load_mat("adj")
            load_mat("w3")
            load_mat("u5")

            def normalise(u, s):
                act.wait_ge(ln_scale_done, u + 1)
                for rc in range(RC):
                    ins = nc.scalar.activation(h0_rows[s][:, rc], x_in[s][:, rc], ACT.Relu,
                                               bias=shift[s][:, rc:rc + 1], scale=inv_std[s][:, rc:rc + 1])
                ins.then_inc(h0_done, 1)

            def first_rows_hi(u, s):
                act.wait_ge(h0_done, u + 1)
                for b in range(GB):
                    part = slice(NC * b, NC * (b + 1))
                    nc.scalar.activation(nat_hi[s][:, part], h0_rows[s][:, part], ACT.Copy).then_inc(nat_hi_done, 1)

            def save_first_turned(u, s):
                for c in range(KC):
                    act.wait_ge(h0_turned, 2 * u + (c + 1))
                    nc.scalar.activation(h0_t[s][:, c], agg_ps[c][:], ACT.Copy).then_inc(h0_t_saved, 1)

            def state_hi_part(source, c, s):
                nc.scalar.activation(state_hi[s][:, c], source[:, c], ACT.Copy).then_inc(state_hi_done, 1)

            def first_state_hi(u, s):
                for c in range(KC):
                    act.wait_ge(h0_t_saved, 2 * u + (c + 1))
                    state_hi_part(h0_t[s], c, s)

            def update_cand(p):
                for c in range(KC):
                    act.wait_ge(cand_mm, count(p, c))
                    nc.scalar.activation(cand[:, c], cand_ps[c][:], ACT.Tanh,
                                         bias=gate_bias[:, 2, c:c + 1]).then_inc(cand_done, 1)

            def slot(q, j, i, first, more):
                s, t = place(j)
                back, back_t = place(j - 1)
                last_step = back_t == STEPS - 1
                for c in range(KC):
                    act.wait_ge(shared_mm, count(q, c))
                    nc.scalar.activation(shared[s][:, c], z_ps[c][:], ACT.Copy).then_inc(shared_saved, 1)
                for c in range(KC):
                    act.wait_ge(agg_mm, count(q, c))
                    nc.scalar.activation(agg_hi[:, c], agg_ps[c][:], ACT.Copy).then_inc(agg_hi_done, 1)
                if not first:
                    update_cand(q - 1)
                for c in range(KC):
                    act.wait_ge(z_mm, count(q, c))
                    nc.scalar.activation(z_gate[s][:, c], z_ps[c][:], ACT.Sigmoid,
                                         bias=gate_bias[:, 0, c:c + 1]).then_inc(z_done, 1)
                if not first and last_step and more:
                    save_first_turned(STREAMS * i + (STREAMS + back), back)
                    first_state_hi(STREAMS * i + (STREAMS + back), back)
                if not first and not last_step:
                    for c in range(KC):
                        act.wait_ge(h_done, count(q - 1, c))
                        state_hi_part(h_t[back], c, back)

                def r_sigmoid(c):
                    act.wait_ge(r_pre_done, count(q, c))
                    nc.scalar.activation(r_gate[:, c], r_pre[:, c], ACT.Sigmoid,
                                         bias=gate_bias[:, 1, c:c + 1]).then_inc(r_done, 1)

                r_sigmoid(0)
                if not first and last_step and more:
                    first_rows_hi(STREAMS * i + (STREAMS + back), back)
                if not first and not last_step:
                    for b in range(GB):
                        act.wait_ge(turned_mm, count(q - 1, b))
                        part = slice(NC * b, NC * (b + 1))
                        nc.scalar.activation(nat_hi[back][:, part], agg_ps[b][:].rearrange("p (c d) -> p c d", c=NC),
                                             ACT.Copy).then_inc(nat_hi_done, 1)
                r_sigmoid(1)
                for c in range(KC):
                    act.wait_ge(rh_done, count(q, c))
                    nc.scalar.activation(rh_hi[:, c], rh[:, c], ACT.Copy).then_inc(rh_hi_done, 1)
                if more and j in (STEPS, STEPS + 1):
                    normalise(STREAMS * i + (STREAMS + j - STEPS), j - STEPS)

            def mat_hi(n):
                for c in range(2):
                    act.wait_ge(mat_turned, 2 * n + c + 1)
                    nc.scalar.activation(hi[MATS[n]][:, c], prep_bank(n, c), ACT.Copy).then_inc(mat_hi_set, 1)

            for s in range(STREAMS):
                normalise(s, s)
                first_rows_hi(s, s)
            save_first_turned(0, 0)
            first_state_hi(0, 0)
            save_first_turned(1, 1)
            first_state_hi(1, 1)
            for n in range(len(MATS)):
                mat_hi(n)
            act.wait_ge(bias_set, 3)
            run_slots(act, slot)
            update_cand(LAST)

        @block.vector
        def _(dve):
            nc.vector.memset(bias_rows[:], 0.0).then_inc(bias_rows_zero, 1)

            def layernorm_stats(s, loads):
                dve.wait_ge(x_loaded[s], 16 * loads)
                for rc in range(RC):
                    ins = nc.vector.bn_stats(stats[s][:, rc], x_in[s][:, rc])
                ins.then_inc(stats_done, 1)

            def layernorm_mean_var(s):
                for rc in range(RC):
                    ins = nc.vector.bn_aggr(mean_var[s][:, rc], stats[s][:, rc])
                ins.then_inc(mean_var_done, 1)

            def first_rows_lo(q, s):
                for b in range(GB):
                    dve.wait_ge(nat_hi_done, count(q, b))
                    part = slice(NC * b, NC * (b + 1))
                    nc.vector.tensor_tensor(nat_lo[s][:, part], h0_rows[s][:, part],
                                            nat_hi[s][:, part].bitcast(F32), ALU.subtract).then_inc(nat_lo_done, 1)

            def state_lo_parts(q, source, s):
                for c in range(KC):
                    dve.wait_ge(state_hi_done, count(q, c))
                    nc.vector.tensor_tensor(state_lo[s][:, c], source[:, c], state_hi[s][:, c].bitcast(F32),
                                            ALU.subtract).then_inc(state_lo_done, 1)

            def update(p, s, t):
                old = h0_t[s] if t == 0 else h_t[s]

                def change_part(c):
                    dve.wait_ge(cand_done, count(p, c))
                    nc.vector.tensor_tensor(change[:, c], cand[:, c], old[:, c], ALU.subtract).then_inc(change_done, 1)

                def gate_part(c):
                    dve.wait_ge(z_done, count(p, c))
                    dve.wait_ge(change_done, count(p, c))
                    nc.vector.tensor_tensor(gated_change[:, c], z_gate[s][:, c], change[:, c],
                                            ALU.mult).then_inc(gated_done, 1)

                def new_part(c):
                    dve.wait_ge(gated_done, count(p, c))
                    nc.vector.tensor_tensor(h_t[s][:, c], old[:, c], gated_change[:, c], ALU.add).then_inc(h_done, 1)

                change_part(0)
                gate_part(0)
                change_part(1)
                new_part(0)
                gate_part(1)
                new_part(1)

            def add_residual(g, p, s, i):
                dve.wait_ge(out_rows_free[s], 16 * i + 16)
                dve.wait_ge(x_kept[s], 16 * i + 16)
                for b in range(GB):
                    dve.wait_ge(turned_mm, count(p, b))
                    part = slice(NC * b, NC * (b + 1))
                    nc.vector.tensor_tensor(out_rows[s][:, part], agg_ps[b][:].rearrange("p (c d) -> p c d", c=NC),
                                            x_kept_rows[s][:, part], ALU.add).then_inc(out_done, 1)

            def slot(q, j, i, first, more):
                s, t = place(j)
                back, back_t = place(j - 1)
                last_step = back_t == STEPS - 1
                for c in range(KC):
                    dve.wait_ge(agg_hi_done, count(q, c))
                    nc.vector.tensor_tensor(agg_lo[:, c], agg_ps[c][:], agg_hi[:, c].bitcast(F32),
                                            ALU.subtract).then_inc(agg_lo_done, 1)
                if not first:
                    update(q - 1, back, back_t)
                    if not last_step:
                        state_lo_parts(q + 1, h_t[back], back)
                    elif more:
                        state_lo_parts(q + 1, h0_t[back], back)
                old = h0_t[s] if t == 0 else h_t[s]
                for c in range(KC):
                    dve.wait_ge(r_mm, count(q, c))
                    dve.wait_ge(shared_saved, count(q, c))
                    nc.vector.tensor_tensor(r_pre[:, c], r_ps[c][:], shared[s][:, c], ALU.add).then_inc(r_pre_done, 1)
                if not first and not last_step:
                    for b in range(GB):
                        dve.wait_ge(nat_hi_done, count(q + 1, b))
                        part = slice(NC * b, NC * (b + 1))
                        nc.vector.tensor_tensor(nat_lo[back][:, part], agg_ps[b][:].rearrange("p (c d) -> p c d", c=NC),
                                                nat_hi[back][:, part].bitcast(F32),
                                                ALU.subtract).then_inc(nat_lo_done, 1)
                if not first and last_step:
                    if more:
                        first_rows_lo(q + 1, back)
                    add_residual(STREAMS * i + back, q - 1, back, i)
                for c in range(KC):
                    dve.wait_ge(r_done, count(q, c))
                    nc.vector.tensor_tensor(rh[:, c], r_gate[:, c], old[:, c], ALU.mult).then_inc(rh_done, 1)
                if more and j in (2, 3):
                    layernorm_stats(j - 2, i + 2)
                    dve.wait_ge(stats_done, STREAMS * i + (STREAMS + j - 1))
                for c in range(KC):
                    dve.wait_ge(rh_hi_done, count(q, c))
                    nc.vector.tensor_tensor(rh_lo[:, c], rh[:, c], rh_hi[:, c].bitcast(F32),
                                            ALU.subtract).then_inc(rh_lo_done, 1)
                if more and j in (2, 3):
                    layernorm_mean_var(j - 2)

            def fold(m):
                dve.wait_ge(mat_loaded[m], 16)
                nc.vector.tensor_tensor(rows[m][:, :, 0:D], rows[m][:, :, 0:D], rows[m][:, :, D:2 * D],
                                        ALU.add).then_inc(folded_sum, 1)

            def mat_lo(n):
                m = MATS[n]
                for c in range(2):
                    dve.wait_ge(mat_hi_set, 2 * n + c + 1)
                    nc.vector.tensor_tensor(lo[m][:, c], prep_bank(n, c), hi[m][:, c].bitcast(F32),
                                            ALU.subtract).then_inc(mat_lo_set, 1)

            for s in range(STREAMS):
                layernorm_stats(s, 1)
                dve.wait_ge(stats_done, s + 1)
                layernorm_mean_var(s)
            for m in folded:
                fold(m)
            for s in range(STREAMS):
                first_rows_lo(s, s)
            for s in range(STREAMS):
                state_lo_parts(s, h0_t[s], s)
            for n in range(len(MATS)):
                mat_lo(n)
            dve.wait_ge(bias_turned, 1)
            nc.vector.tensor_copy(bias_cols[:], agg_ps[0][:, 0:10]).then_inc(bias_copied, 1)
            dve.wait_ge(bias_copied, 1)
            for gate, (a, b) in enumerate(((0, 1), (2, 1), (3, 4))):
                nc.vector.tensor_tensor(gate_bias[:, gate], bias_cols[:, KC * a:KC * (a + 1)],
                                        bias_cols[:, KC * b:KC * (b + 1)], ALU.add).then_inc(bias_set, 1)
            run_slots(dve, slot)
            update(LAST, *place(TPR - 1))
            add_residual(GROUPS - 1, LAST, STREAMS - 1, ROUNDS - 1)

        @block.tensor
        def _(pe):
            def product(bank, m, o, part_hi, part_lo, hi_ready, lo_ready, opens, closed):
                rows_o = slice(P * o, P * (o + 1))
                for k in range(KC):
                    hi_ready(k)
                    pe.matmul(bank[:], hi[m][:, k, rows_o], part_hi[:, k], start=opens and k == 0, stop=False,
                              skip_group_check=True)
                    pe.matmul(bank[:], lo[m][:, k, rows_o], part_hi[:, k], start=False, stop=False,
                              skip_group_check=True)
                for k in range(KC):
                    lo_ready(k)
                    mm = pe.matmul(bank[:], hi[m][:, k, rows_o], part_lo[:, k], start=False, stop=k == KC - 1,
                                   skip_group_check=True)
                if closed is not None:
                    mm.then_inc(closed, 1)

            def waits(signal, q, o):
                return lambda k: pe.wait_ge(signal, count(q, k)) if o == 0 else None

            def shared_product(q, s, first):
                for o in range(KC):
                    if not first:
                        pe.wait_ge(z_done, count(q - 1, o))
                    product(z_ps[o], "u3", o, state_hi[s], state_lo[s], waits(state_hi_done, q, o),
                            waits(state_lo_done, q, o), True, shared_mm)

            def aggregate(q, s):
                for d in range(KC):
                    cols_d = slice(P * d, P * (d + 1))
                    for b in range(GB):
                        dst = agg_ps[d][:, N * b:N * (b + 1)]
                        if d == 0:
                            pe.wait_ge(nat_lo_done, count(q, b))
                        for c in range(NC):
                            rc = NC * b + c
                            pe.matmul(dst, nat_hi[s][:, rc, cols_d], hi["adj"][:, c], start=c == 0, stop=False)
                            pe.matmul(dst, nat_hi[s][:, rc, cols_d], lo["adj"][:, c], start=False, stop=False)
                        for c in range(NC):
                            rc = NC * b + c
                            mm = pe.matmul(dst, nat_lo[s][:, rc, cols_d], hi["adj"][:, c], start=False,
                                           stop=c == NC - 1)
                    mm.then_inc(agg_mm, 1)

            def close_cand(p):
                for o in range(KC):
                    product(cand_ps[o], "u5", o, rh_hi, rh_lo, waits(rh_hi_done, p, o), waits(rh_lo_done, p, o),
                            False, cand_mm)

            def turn_state(p, s):
                for k in range(KC):
                    pe.wait_ge(h_done, count(p, k))
                    for b in range(GB):
                        for c in range(NC):
                            at = D * c + P * k
                            mm = pe.transpose(agg_ps[b][:, at:at + P],
                                              h_t[s][:, k, N * b + P * c:N * b + P * (c + 1)], identity[:])
                        if k == KC - 1:
                            mm.then_inc(turned_mm, 1)

            def turn_first(u, s):
                pe.wait_ge(h0_done, u + 1)
                for k in range(KC):
                    for rc in range(RC):
                        mm = pe.transpose(agg_ps[k][:, P * rc:P * (rc + 1)], h0_rows[s][:, rc, P * k:P * (k + 1)],
                                          identity[:])
                    mm.then_inc(h0_turned, 1)

            def slot(q, j, i, first, more):
                s, t = place(j)
                back, back_t = place(j - 1)
                last_step = back_t == STEPS - 1
                shared_product(q, s, first)
                aggregate(q, s)
                if not first:
                    close_cand(q - 1)
                for o in range(KC):
                    pe.wait_ge(shared_saved, count(q, o))
                    product(z_ps[o], "w3", o, agg_hi, agg_lo, waits(agg_hi_done, q, o), waits(agg_lo_done, q, o),
                            False, z_mm)
                if not first and last_step and more:
                    turn_first(STREAMS * i + (STREAMS + back), back)
                for o in range(KC):
                    if not first:
                        pe.wait_ge(r_pre_done, count(q - 1, o))
                    product(r_ps[o], "w4", o, agg_hi, agg_lo, waits(agg_hi_done, q, o), waits(agg_lo_done, q, o),
                            True, r_mm)
                if not first:
                    if last_step and more:
                        pe.wait_ge(h0_t_saved, 2 * (STREAMS * i + (STREAMS + back)) + 2)
                    turn_state(q - 1, back)
                for o in range(KC):
                    if not first:
                        pe.wait_ge(cand_done, count(q - 1, o))
                    product(cand_ps[o], "w5", o, agg_hi, agg_lo, waits(agg_hi_done, q, o),
                            waits(agg_lo_done, q, o), True, None)
                if not first and last_step:
                    pe.wait_ge(out_done, 2 * (STREAMS * i + back) + 2)

            pe.wait_ge(identity_set, 1)
            for u in range(STREAMS):
                if u:
                    pe.wait_ge(h0_t_saved, 2 * u)
                turn_first(u, u)
            for n, m in enumerate(MATS):
                if m in folded:
                    pe.wait_ge(folded_sum, folded.index(m) + 1)
                else:
                    pe.wait_ge(mat_loaded[m], 16)
                if n >= 3:
                    pe.wait_ge(mat_lo_set, 2 * (n - 3) + 2)
                for k in range(2):
                    for o in range(2):
                        mm = pe.transpose(prep_bank(n, k)[:, P * o:P * (o + 1)], rows[m][:, o, P * k:P * (k + 1)],
                                          identity[:])
                    mm.then_inc(mat_turned, 1)
            pe.wait_ge(bias_loaded, 80)
            pe.wait_ge(h0_t_saved, 2 * STREAMS)
            pe.transpose(agg_ps[0][:, 0:P], bias_rows[:], identity[:]).then_inc(bias_turned, 1)
            pe.wait_ge(bias_copied, 1)
            pe.wait_ge(mat_lo_set, 2 * len(MATS))
            run_slots(pe, slot)
            close_cand(LAST)
            pe.wait_ge(agg_lo_done, count(LAST, KC - 1))
            turn_state(LAST, STREAMS - 1)


_INS = ["x", "adj", "L0_gnn_w3_w", "L0_gnn_w3_b", "L0_gnn_u3_w", "L0_gnn_u3_b", "L0_gnn_w4_w", "L0_gnn_w4_b",
        "L0_gnn_w5_w", "L0_gnn_w5_b", "L0_gnn_u5_w", "L0_gnn_u5_b"]


def kernel(**inputs):
    import numpy as _np
    import concourse.bacc as _bacc
    from concourse import mybir as _mybir
    from concourse.bass_utils import run_bass_kernel_spmd as _run

    nc = _bacc.Bacc("TRN2", target_bir_lowering=False, num_devices=1)
    arrays, args = {}, []
    for name in _INS:
        a = _np.ascontiguousarray(inputs[name])
        arrays[f"in_{name}_dram"] = a
        args.append(nc.dram_tensor(f"in_{name}_dram", a.shape, _mybir.dt.from_np(a.dtype), kind="ExternalInput").ap())
    out = nc.dram_tensor("out_0_dram", inputs["x"].shape, _mybir.dt.float32, kind="ExternalOutput").ap()
    gated_graph_network(nc, *args, out)
    r = _run(nc, [arrays], core_ids=[0])
    return r.results[0]["out_0_dram"]
```

```python
from contextlib import ExitStack

import concourse.bass as bass
from concourse import mybir

F32 = mybir.dt.float32
F32R = mybir.dt.float32r
ALU = mybir.AluOpType
ACT = mybir.ActivationFunctionType

P = 128
EPS = 1e-5
STEPS = 3
STREAMS = 2


def gated_graph_network(nc, x, adj, w3_w, w3_b, u3_w, u3_b, w4_w, w4_b, w5_w, w5_b, u5_w, u5_b, out):
    B, N, D = x.shape
    KC = D // P
    NC = N // P
    GB = 2
    COLS = GB * N
    RC = GB * NC
    GROUPS = B // GB
    ROUNDS = GROUPS // STREAMS
    TPR = STEPS * STREAMS
    assert KC == 2 and NC == 2 and COLS == 512 and GROUPS % STREAMS == 0 and STREAMS == 2

    x_groups = x.rearrange("(g b) (c p) d -> g p b c d", b=GB, p=P)
    out_groups = out.rearrange("(g b) (c p) d -> g p b c d", b=GB, p=P)

    with ExitStack() as ctx:
        def sb(name, shape, dt=F32):
            return ctx.enter_context(nc.sbuf_tensor(name, shape, dt))

        def sem(name):
            return ctx.enter_context(nc.semaphore(name))

        def per_stream(name, shape, dt=F32):
            return [sb(f"{name}{s}", shape, dt) for s in range(STREAMS)]

        MATS = ("adj", "u3", "w3", "w4", "w5", "u5")
        sources = {"adj": adj, "u3": u3_w, "w3": w3_w, "w4": w4_w, "w5": w5_w, "u5": u5_w}
        folded = ("w3", "w4", "w5")
        rows = {m: sb(f"rows_{m}", [P, 2, sources[m].shape[1]]) for m in MATS}
        hi = {m: sb(f"{m}_hi", [P, 2, 256], F32R) for m in MATS}
        lo = {m: sb(f"{m}_lo", [P, 2, 256], F32R) for m in MATS}
        identity = sb("identity", [P, P])
        bias_rows = sb("bias_rows", [P, P])
        bias_cols = sb("bias_cols", [P, 10])
        gate_bias = sb("gate_bias", [P, 4, KC])
        table_warm = sb("table_warm", [P, 1])
        eps_tile = sb("eps_tile", [P, RC])
        minus_half = sb("minus_half", [P, RC])
        minus_one = sb("minus_one", [P, RC])

        x_in = per_stream("x_in", [P, RC, D])
        x_kept_rows = per_stream("x_kept_rows", [P, RC, D])
        out_rows = per_stream("out_rows", [P, RC, D])
        stats = per_stream("stats", [P, RC, 6])
        mean_var = per_stream("mean_var", [P, RC, 2])
        var_eps = per_stream("var_eps", [P, RC])
        inv_std = per_stream("inv_std", [P, RC])
        mean_scaled = per_stream("mean_scaled", [P, RC])
        shift = per_stream("shift", [P, RC])
        h0_rows = per_stream("h0_rows", [P, RC, D])
        nat_hi = per_stream("nat_hi", [P, RC, D], F32R)
        nat_lo = per_stream("nat_lo", [P, RC, D], F32R)
        h0_t = per_stream("h0_t", [P, KC, COLS])
        h_t = per_stream("h_t", [P, KC, COLS])
        state_hi = per_stream("state_hi", [P, KC, COLS], F32R)
        state_lo = per_stream("state_lo", [P, KC, COLS], F32R)
        shared = per_stream("shared", [P, KC, COLS])
        z_gate = per_stream("z_gate", [P, KC, COLS])
        not_z = sb("not_z", [P, KC, COLS])
        kept_h = per_stream("kept_h", [P, KC, COLS])
        agg_hi = sb("agg_hi", [P, KC, COLS], F32R)
        agg_lo = sb("agg_lo", [P, KC, COLS], F32R)
        r_pre = sb("r_pre", [P, KC, COLS])
        r_gate = sb("r_gate", [P, KC, COLS])
        rh = sb("rh", [P, KC, COLS])
        rh_hi = sb("rh_hi", [P, KC, COLS], F32R)
        rh_lo = sb("rh_lo", [P, KC, COLS], F32R)
        cand = sb("cand", [P, KC, COLS])
        z_cand = sb("z_cand", [P, KC, COLS])

        def bank_pair(name):
            return [ctx.enter_context(nc.psum_tensor(f"{name}{c}", [P, 512], F32)) for c in range(2)]

        agg_ps = bank_pair("agg_ps")
        z_ps = bank_pair("z_ps")
        r_ps = bank_pair("r_ps")
        cand_ps = bank_pair("cand_ps")

        mat_loaded = {m: sem(f"{m}_loaded") for m in MATS}
        bias_loaded = sem("bias_loaded")
        x_loaded = [sem(f"x_loaded{s}") for s in range(STREAMS)]
        out_rows_free = [sem(f"out_rows_free{s}") for s in range(STREAMS)]
        consts_set = sem("consts_set")
        blank_set = sem("blank_set")
        identity_set = sem("identity_set")
        folded_sum = sem("folded_sum")
        mat_turned = sem("mat_turned")
        mat_hi_set = sem("mat_hi_set")
        mat_lo_set = sem("mat_lo_set")
        bias_turned = sem("bias_turned")
        bias_copied = sem("bias_copied")
        bias_set = sem("bias_set")
        stats_done = sem("stats_done")
        mean_var_done = sem("mean_var_done")
        ln_chain = sem("ln_chain")
        ln_scale_done = sem("ln_scale_done")
        h0_done = sem("h0_done")
        h0_turned = sem("h0_turned")
        h0_t_saved = sem("h0_t_saved")
        x_kept = [sem(f"x_kept{s}") for s in range(STREAMS)]
        out_done = sem("out_done")
        shared_mm = sem("shared_mm")
        agg_mm = sem("agg_mm")
        z_mm = sem("z_mm")
        r_mm = sem("r_mm")
        cand_mm = sem("cand_mm")
        turned_mm = sem("turned_mm")
        shared_saved = sem("shared_saved")
        agg_hi_done = sem("agg_hi_done")
        agg_lo_done = sem("agg_lo_done")
        z_done = sem("z_done")
        r_pre_done = sem("r_pre_done")
        r_done = sem("r_done")
        rh_done = sem("rh_done")
        rh_hi_done = sem("rh_hi_done")
        rh_lo_done = sem("rh_lo_done")
        cand_done = sem("cand_done")
        kept_done = sem("kept_done")
        z_cand_done = sem("z_cand_done")
        h_done = sem("h_done")
        state_hi_done = sem("state_hi_done")
        state_lo_done = sem("state_lo_done")
        nat_hi_done = sem("nat_hi_done")
        nat_lo_done = sem("nat_lo_done")

        def count(q, c):
            return 2 * q + (c + 1)

        def whole(q):
            return q + 1

        def run_slots(eng, slot):
            slot(0, 0, -1, True, True)
            slot(1, 1, 0, False, True)
            with nc.Fori(0, ROUNDS - 1, engines=(eng.engine,), hint_back_edge=True) as i:
                for j in range(STREAMS, TPR + STREAMS):
                    slot(TPR * i + j, j, i, False, True)
            for j in range(STREAMS, TPR):
                slot(TPR * (ROUNDS - 1) + j, j, ROUNDS - 1, False, False)

        LAST = TPR * ROUNDS - 1

        def place(j):
            return j % STREAMS, (j // STREAMS) % STEPS

        def prep_bank(n, c):
            return (z_ps, r_ps, cand_ps, r_ps, cand_ps, agg_ps)[n][c][:, 0:256]

        block = ctx.enter_context(nc.Block())

        @block.sync
        def _(sp):
            def load_x(g, s):
                sp.dma_start(x_in[s][:].rearrange("p (b c) d -> p b c d", b=GB),
                             x_groups[g]).then_inc(x_loaded[s], 16)

            def load_mat(m):
                sp.dma_start(rows[m][:], sources[m].rearrange("(c p) k -> p c k", p=P)).then_inc(mat_loaded[m], 16)

            for s in range(STREAMS):
                sp.sem_inc(out_rows_free[s], 16)
            load_x(0, 0)
            load_mat("u3")
            sp.wait_ge(blank_set, 2)
            for n, b in enumerate((w3_b, u3_b, w4_b, w5_b, u5_b)):
                sp.dma_start(bias_rows[KC * n:KC * (n + 1), :], b.rearrange("(c p) -> c p", p=P)
                             ).then_inc(bias_loaded, 16)
            load_mat("w4")
            load_x(1, 1)
            load_mat("w5")
            load_mat("u5")

            def keep_x(s, i):
                sp.wait_ge(x_loaded[s], 16 * i + 16)
                sp.dma_start(x_kept_rows[s][:], x_in[s][:]).then_inc(x_kept[s], 16)

            def refill(g, s, i):
                sp.wait_ge(mean_var_done, g - 1)
                sp.wait_ge(h0_done, g - 1)
                sp.wait_ge(x_kept[s], 16 * i)
                load_x(g, s)

            def store(g, s):
                sp.wait_ge(out_done, 2 * g + 2)
                sp.dma_start(out_groups[g], out_rows[s][:].rearrange("p (b c) d -> p b c d", b=GB)
                             ).then_inc(out_rows_free[s], 16)

            for s in range(STREAMS):
                keep_x(s, 0)
                refill(STREAMS + s, s, 1)
            with sp.Fori(0, ROUNDS - 2) as i:
                for s in range(STREAMS):
                    store(STREAMS * i + s, s)
                    keep_x(s, i + 1)
                    refill(STREAMS * i + (2 * STREAMS + s), s, i + 2)
            for s in range(STREAMS):
                store(STREAMS * (ROUNDS - 2) + s, s)
                keep_x(s, ROUNDS - 1)
            store(GROUPS - 2, 0)
            for b in range(GB):
                sp.wait_ge(out_done, 2 * (GROUPS - 1) + b + 1)
                sp.dma_start(out_groups[GROUPS - 1][:, b], out_rows[1][:, NC * b:NC * (b + 1)]
                             ).then_inc(out_rows_free[1], 16)
            for s in range(STREAMS):
                sp.wait_ge(out_rows_free[s], 16 * (ROUNDS + s) + 16)

        @block.gpsimd
        def _(pool):
            nc.gpsimd.memset(identity[:], 0.0).then_inc(consts_set, 1)
            nc.gpsimd.memset(eps_tile[:], EPS).then_inc(consts_set, 1)
            nc.gpsimd.memset(minus_half[:], -0.5).then_inc(consts_set, 1)
            nc.gpsimd.memset(minus_one[:], -1.0).then_inc(consts_set, 1)
            pool.wait_ge(consts_set, 4)
            nc.gpsimd.affine_select(out=identity[:], in_=identity[:], compare_op=ALU.not_equal, fill=1.0,
                                    base=0, pattern=[[-1, P]], channel_multiplier=1).then_inc(identity_set, 1)

            def ln_scale(u, s):
                pool.wait_ge(mean_var_done, u + 1)
                nc.gpsimd.tensor_tensor(var_eps[s][:], mean_var[s][:, :, 1], eps_tile[:], ALU.add).then_inc(ln_chain, 1)
                pool.wait_ge(ln_chain, 3 * u + 1)
                nc.gpsimd.tensor_tensor(inv_std[s][:], var_eps[s][:], minus_half[:], ALU.pow).then_inc(ln_chain, 1)
                pool.wait_ge(ln_chain, 3 * u + 2)
                nc.gpsimd.tensor_tensor(mean_scaled[s][:], mean_var[s][:, :, 0], inv_std[s][:],
                                        ALU.mult).then_inc(ln_chain, 1)
                pool.wait_ge(ln_chain, 3 * u + 3)
                nc.gpsimd.tensor_tensor(shift[s][:], mean_scaled[s][:], minus_one[:],
                                        ALU.mult).then_inc(ln_scale_done, 1)

            for s in range(STREAMS):
                ln_scale(s, s)
            with pool.Fori(1, ROUNDS) as i:
                for s in range(STREAMS):
                    ln_scale(STREAMS * i + s, s)

        @block.scalar
        def _(act):
            def load_mat(m):
                act.dma_start(rows[m][:], sources[m].rearrange("(c p) k -> p c k", p=P)).then_inc(mat_loaded[m], 16)

            load_mat("adj")
            load_mat("w3")
            act.wait_ge(blank_set, 1)
            nc.scalar.activation(table_warm[:], table_warm[:], ACT.Sigmoid)

            def normalise(u, s):
                act.wait_ge(ln_scale_done, u + 1)
                for rc in range(RC):
                    ins = nc.scalar.activation(h0_rows[s][:, rc], x_in[s][:, rc], ACT.Relu,
                                               bias=shift[s][:, rc:rc + 1], scale=inv_std[s][:, rc:rc + 1])
                ins.then_inc(h0_done, 1)

            def first_rows_hi(u, s):
                act.wait_ge(h0_done, u + 1)
                for b in range(GB):
                    part = slice(NC * b, NC * (b + 1))
                    nc.scalar.activation(nat_hi[s][:, part], h0_rows[s][:, part], ACT.Copy).then_inc(nat_hi_done, 1)

            def save_first_turned(u, s):
                for c in range(KC):
                    act.wait_ge(h0_turned, 2 * u + (c + 1))
                    nc.scalar.activation(h0_t[s][:, c], agg_ps[c][:], ACT.Copy).then_inc(h0_t_saved, 1)

            def state_hi_whole(source, s):
                nc.scalar.activation(state_hi[s][:], source[:], ACT.Copy).then_inc(state_hi_done, 1)

            def first_state_hi(u, s):
                act.wait_ge(h0_t_saved, 2 * u + 2)
                state_hi_whole(h0_t[s], s)

            def update_cand(p):
                for c in range(KC):
                    act.wait_ge(cand_mm, count(p, c))
                    nc.scalar.activation(cand[:, c], cand_ps[c][:], ACT.Tanh,
                                         bias=gate_bias[:, 2, c:c + 1]).then_inc(cand_done, 1)

            def slot(q, j, i, first, more):
                s, t = place(j)
                back, back_t = place(j - 1)
                last_step = back_t == STEPS - 1
                for c in range(KC):
                    act.wait_ge(shared_mm, count(q, c))
                    nc.scalar.activation(shared[s][:, c], z_ps[c][:], ACT.Copy).then_inc(shared_saved, 1)
                for c in range(KC):
                    act.wait_ge(agg_mm, count(q, c))
                    nc.scalar.activation(agg_hi[:, c], agg_ps[c][:], ACT.Copy).then_inc(agg_hi_done, 1)
                if not first:
                    update_cand(q - 1)

                def z_sigmoids(c):
                    act.wait_ge(z_mm, count(q, c))
                    nc.scalar.activation(z_gate[s][:, c], z_ps[c][:], ACT.Sigmoid,
                                         bias=gate_bias[:, 0, c:c + 1])
                    nc.scalar.activation(not_z[:, c], z_ps[c][:], ACT.Sigmoid, scale=-1.0,
                                         bias=gate_bias[:, 3, c:c + 1]).then_inc(z_done, 1)

                if not first:
                    act.wait_ge(kept_done, whole(q - 1))
                z_sigmoids(0)
                if not last_step:
                    act.wait_ge(h_done, count(q - 1, KC - 1))
                    state_hi_whole(h_t[back], back)
                z_sigmoids(1)
                if last_step and more:
                    save_first_turned(STREAMS * i + (STREAMS + back), back)
                    first_state_hi(STREAMS * i + (STREAMS + back), back)

                def r_sigmoid(c):
                    act.wait_ge(r_pre_done, count(q, c))
                    nc.scalar.activation(r_gate[:, c], r_pre[:, c], ACT.Sigmoid,
                                         bias=gate_bias[:, 1, c:c + 1]).then_inc(r_done, 1)

                r_sigmoid(0)
                if last_step and more:
                    first_rows_hi(STREAMS * i + (STREAMS + back), back)
                if not last_step:
                    for b in range(GB):
                        act.wait_ge(turned_mm, count(q - 1, b))
                        part = slice(NC * b, NC * (b + 1))
                        nc.scalar.activation(nat_hi[back][:, part], agg_ps[b][:].rearrange("p (c d) -> p c d", c=NC),
                                             ACT.Copy).then_inc(nat_hi_done, 1)
                r_sigmoid(1)
                for c in range(KC):
                    act.wait_ge(rh_done, count(q, c))
                    nc.scalar.activation(rh_hi[:, c], rh[:, c], ACT.Copy).then_inc(rh_hi_done, 1)
                if more and j in (STEPS, STEPS + 1):
                    normalise(STREAMS * i + (STREAMS + j - STEPS), j - STEPS)

            def mat_hi(n):
                for c in range(2):
                    act.wait_ge(mat_turned, 2 * n + c + 1)
                    nc.scalar.activation(hi[MATS[n]][:, c], prep_bank(n, c), ACT.Copy).then_inc(mat_hi_set, 1)

            for n in range(3):
                mat_hi(n)
            normalise(0, 0)
            mat_hi(3)
            save_first_turned(0, 0)
            first_state_hi(0, 0)
            for n in range(4, len(MATS)):
                mat_hi(n)
            first_rows_hi(0, 0)
            normalise(1, 1)
            act.wait_ge(bias_set, 4)
            run_slots(act, slot)
            update_cand(LAST)

        @block.vector
        def _(dve):
            nc.vector.memset(table_warm[:], 0.0).then_inc(blank_set, 1)
            nc.vector.memset(bias_rows[:], 0.0).then_inc(blank_set, 1)

            def layernorm_stats(s, loads):
                dve.wait_ge(x_loaded[s], 16 * loads)
                for rc in range(RC):
                    ins = nc.vector.bn_stats(stats[s][:, rc], x_in[s][:, rc])
                ins.then_inc(stats_done, 1)

            def layernorm_mean_var(s):
                for rc in range(RC):
                    ins = nc.vector.bn_aggr(mean_var[s][:, rc], stats[s][:, rc])
                ins.then_inc(mean_var_done, 1)

            def first_rows_lo(q, s):
                for b in range(GB):
                    dve.wait_ge(nat_hi_done, count(q, b))
                    part = slice(NC * b, NC * (b + 1))
                    nc.vector.tensor_tensor(nat_lo[s][:, part], h0_rows[s][:, part],
                                            nat_hi[s][:, part].bitcast(F32), ALU.subtract).then_inc(nat_lo_done, 1)

            def state_lo_whole(q, source, s):
                dve.wait_ge(state_hi_done, whole(q))
                nc.vector.tensor_tensor(state_lo[s][:], source[:], state_hi[s][:].bitcast(F32),
                                        ALU.subtract).then_inc(state_lo_done, 1)

            def keep_part_of_h(q, s, old):
                dve.wait_ge(z_done, count(q, KC - 1))
                nc.vector.tensor_tensor(kept_h[s][:], not_z[:], old[:], ALU.mult).then_inc(kept_done, 1)

            def update(p, s):
                def gated(c):
                    dve.wait_ge(cand_done, count(p, c))
                    nc.vector.tensor_tensor(z_cand[:, c], z_gate[s][:, c], cand[:, c], ALU.mult).then_inc(z_cand_done, 1)

                def new(c):
                    dve.wait_ge(kept_done, whole(p))
                    dve.wait_ge(z_cand_done, count(p, c))
                    nc.vector.tensor_tensor(h_t[s][:, c], kept_h[s][:, c], z_cand[:, c], ALU.add).then_inc(h_done, 1)

                gated(0)
                new(0)
                gated(1)
                new(1)

            def add_residual(g, p, s, i, banks=agg_ps):
                dve.wait_ge(out_rows_free[s], 16 * i + 16)
                dve.wait_ge(x_kept[s], 16 * i + 16)
                for b in range(GB):
                    dve.wait_ge(turned_mm, count(p, b))
                    part = slice(NC * b, NC * (b + 1))
                    nc.vector.tensor_tensor(out_rows[s][:, part], banks[b][:].rearrange("p (c d) -> p c d", c=NC),
                                            x_kept_rows[s][:, part], ALU.add).then_inc(out_done, 1)

            def slot(q, j, i, first, more):
                s, t = place(j)
                back, back_t = place(j - 1)
                last_step = back_t == STEPS - 1
                for c in range(KC):
                    dve.wait_ge(agg_hi_done, count(q, c))
                    nc.vector.tensor_tensor(agg_lo[:, c], agg_ps[c][:], agg_hi[:, c].bitcast(F32),
                                            ALU.subtract).then_inc(agg_lo_done, 1)
                if not first:
                    update(q - 1, back)
                old = h0_t[s] if t == 0 else h_t[s]

                def r_sum(c):
                    dve.wait_ge(r_mm, count(q, c))
                    dve.wait_ge(shared_saved, count(q, c))
                    nc.vector.tensor_tensor(r_pre[:, c], r_ps[c][:], shared[s][:, c], ALU.add).then_inc(r_pre_done, 1)

                if not last_step:
                    state_lo_whole(q + 1, h_t[back], back)
                r_sum(0)
                if last_step and more:
                    state_lo_whole(q + 1, h0_t[back], back)
                r_sum(1)
                if not first and last_step and more:
                    add_residual(STREAMS * i + back, q - 1, back, i)
                if not last_step:
                    for b in range(GB):
                        dve.wait_ge(nat_hi_done, count(q + 1, b))
                        part = slice(NC * b, NC * (b + 1))
                        nc.vector.tensor_tensor(nat_lo[back][:, part], agg_ps[b][:].rearrange("p (c d) -> p c d", c=NC),
                                                nat_hi[back][:, part].bitcast(F32),
                                                ALU.subtract).then_inc(nat_lo_done, 1)
                for c in range(KC):
                    dve.wait_ge(r_done, count(q, c))
                    nc.vector.tensor_tensor(rh[:, c], r_gate[:, c], old[:, c], ALU.mult).then_inc(rh_done, 1)
                if last_step and more:
                    first_rows_lo(q + 1, back)
                if more and j in (2, 3):
                    layernorm_stats(j - 2, i + 2)
                    dve.wait_ge(stats_done, STREAMS * i + (STREAMS + j - 1))
                dve.wait_ge(rh_hi_done, count(q, KC - 1))
                nc.vector.tensor_tensor(rh_lo[:], rh[:], rh_hi[:].bitcast(F32), ALU.subtract).then_inc(rh_lo_done, 1)
                keep_part_of_h(q, s, old)
                if not first and last_step and not more:
                    add_residual(STREAMS * i + back, q - 1, back, i)
                if more and j in (2, 3):
                    layernorm_mean_var(j - 2)

            def fold(m):
                dve.wait_ge(mat_loaded[m], 16)
                nc.vector.tensor_tensor(rows[m][:, :, 0:D], rows[m][:, :, 0:D], rows[m][:, :, D:2 * D],
                                        ALU.add).then_inc(folded_sum, 1)

            def mat_lo(n):
                m = MATS[n]
                for c in range(2):
                    dve.wait_ge(mat_hi_set, 2 * n + c + 1)
                    nc.vector.tensor_tensor(lo[m][:, c], prep_bank(n, c), hi[m][:, c].bitcast(F32),
                                            ALU.subtract).then_inc(mat_lo_set, 1)

            def first_stats(s):
                layernorm_stats(s, 1)
                dve.wait_ge(stats_done, s + 1)
                layernorm_mean_var(s)

            def sum_biases():
                dve.wait_ge(bias_turned, 1)
                nc.vector.tensor_copy(bias_cols[:], agg_ps[0][:, 0:10]).then_inc(bias_copied, 1)
                dve.wait_ge(bias_copied, 1)
                for gate, (a, b) in enumerate(((0, 1), (2, 1), (3, 4))):
                    nc.vector.tensor_tensor(gate_bias[:, gate], bias_cols[:, KC * a:KC * (a + 1)],
                                            bias_cols[:, KC * b:KC * (b + 1)], ALU.add).then_inc(bias_set, 1)
                dve.wait_ge(bias_set, 3)
                nc.vector.tensor_scalar(gate_bias[:, 3], gate_bias[:, 0], -1.0, None, ALU.mult).then_inc(bias_set, 1)

            first_stats(0)
            fold("w3")
            for n in range(3):
                mat_lo(n)
            sum_biases()
            fold("w4")
            mat_lo(3)
            first_stats(1)
            fold("w5")
            state_lo_whole(0, h0_t[0], 0)
            for n in range(4, len(MATS)):
                mat_lo(n)
            first_rows_lo(0, 0)
            run_slots(dve, slot)
            update(LAST, STREAMS - 1)
            add_residual(GROUPS - 1, LAST, STREAMS - 1, ROUNDS - 1, z_ps)

        @block.tensor
        def _(pe):
            def product(bank, m, o, part_hi, part_lo, hi_ready, lo_ready, opens, closed):
                rows_o = slice(P * o, P * (o + 1))
                for k in range(KC):
                    hi_ready(k)
                    pe.matmul(bank[:], lo[m][:, k, rows_o], part_hi[:, k], start=opens and k == 0, stop=False,
                              skip_group_check=True)
                    pe.matmul(bank[:], hi[m][:, k, rows_o], part_hi[:, k], start=False, stop=False,
                              skip_group_check=True)
                    lo_ready(k)
                    mm = pe.matmul(bank[:], hi[m][:, k, rows_o], part_lo[:, k], start=False, stop=k == KC - 1,
                                   skip_group_check=True)
                if closed is not None:
                    mm.then_inc(closed, 1)

            def waits(signal, q, o):
                return lambda k: pe.wait_ge(signal, count(q, k)) if o == 0 else None

            def wait_whole(signal, q, o):
                return lambda k: pe.wait_ge(signal, whole(q)) if o == 0 and k == 0 else None

            def shared_product(q, s, first):
                for o in range(KC):
                    if not first:
                        pe.wait_ge(z_done, count(q - 1, o))
                    product(z_ps[o], "u3", o, state_hi[s], state_lo[s], wait_whole(state_hi_done, q, o),
                            wait_whole(state_lo_done, q, o), True, shared_mm)

            def aggregate(q, s):
                for d in range(KC):
                    cols_d = slice(P * d, P * (d + 1))
                    for b in range(GB):
                        dst = agg_ps[d][:, N * b:N * (b + 1)]
                        if d == 0:
                            pe.wait_ge(nat_lo_done, count(q, b))
                        for c in range(NC):
                            rc = NC * b + c
                            pe.matmul(dst, nat_hi[s][:, rc, cols_d], hi["adj"][:, c], start=c == 0, stop=False)
                            pe.matmul(dst, nat_hi[s][:, rc, cols_d], lo["adj"][:, c], start=False, stop=False)
                        for c in range(NC):
                            rc = NC * b + c
                            mm = pe.matmul(dst, nat_lo[s][:, rc, cols_d], hi["adj"][:, c], start=False,
                                           stop=c == NC - 1)
                    mm.then_inc(agg_mm, 1)

            def close_cand(p):
                for o in range(KC):
                    product(cand_ps[o], "u5", o, rh_hi, rh_lo, waits(rh_hi_done, p, o), wait_whole(rh_lo_done, p, o),
                            False, cand_mm)

            def turn_state(p, s, banks):
                for k in range(KC):
                    pe.wait_ge(h_done, count(p, k))
                    for b in range(GB):
                        for c in range(NC):
                            at = D * c + P * k
                            mm = pe.transpose(banks[b][:, at:at + P],
                                              h_t[s][:, k, N * b + P * c:N * b + P * (c + 1)], identity[:])
                        if k == KC - 1:
                            mm.then_inc(turned_mm, 1)

            def turn_first(u, s):
                pe.wait_ge(h0_done, u + 1)
                for k in range(KC):
                    for rc in range(RC):
                        mm = pe.transpose(agg_ps[k][:, P * rc:P * (rc + 1)], h0_rows[s][:, rc, P * k:P * (k + 1)],
                                          identity[:])
                    mm.then_inc(h0_turned, 1)

            def slot(q, j, i, first, more):
                s, t = place(j)
                back, back_t = place(j - 1)
                last_step = back_t == STEPS - 1
                shared_product(q, s, first)
                if j >= TPR:
                    pe.wait_ge(out_done, 2 * (STREAMS * i + s) + 2)
                if first:
                    pe.wait_ge(mat_lo_set, 2 * len(MATS))
                aggregate(q, s)
                if not first:
                    close_cand(q - 1)
                for o in range(KC):
                    pe.wait_ge(shared_saved, count(q, o))
                    product(z_ps[o], "w3", o, agg_hi, agg_lo, waits(agg_hi_done, q, o), waits(agg_lo_done, q, o),
                            False, z_mm)
                if last_step and more:
                    turn_first(STREAMS * i + (STREAMS + back), back)
                for o in range(KC):
                    if not first:
                        pe.wait_ge(r_pre_done, count(q - 1, o))
                    product(r_ps[o], "w4", o, agg_hi, agg_lo, waits(agg_hi_done, q, o), waits(agg_lo_done, q, o),
                            True, r_mm)
                if not first:
                    if last_step and more:
                        pe.wait_ge(h0_t_saved, 2 * (STREAMS * i + (STREAMS + back)) + 2)
                    turn_state(q - 1, back, agg_ps)
                for o in range(KC):
                    if not first:
                        pe.wait_ge(cand_done, count(q - 1, o))
                    product(cand_ps[o], "w5", o, agg_hi, agg_lo, waits(agg_hi_done, q, o),
                            waits(agg_lo_done, q, o), True, None)
            pe.wait_ge(identity_set, 1)

            def turn_mat(n):
                m = MATS[n]
                if m in folded:
                    pe.wait_ge(folded_sum, folded.index(m) + 1)
                else:
                    pe.wait_ge(mat_loaded[m], 16)
                for k in range(2):
                    for o in range(2):
                        mm = pe.transpose(prep_bank(n, k)[:, P * o:P * (o + 1)], rows[m][:, o, P * k:P * (k + 1)],
                                          identity[:])
                    mm.then_inc(mat_turned, 1)

            for n in range(3):
                turn_mat(n)
            pe.wait_ge(bias_loaded, 80)
            pe.transpose(agg_ps[0][:, 0:P], bias_rows[:], identity[:]).then_inc(bias_turned, 1)
            pe.wait_ge(mat_lo_set, 4)
            turn_mat(3)
            pe.wait_ge(bias_copied, 1)
            turn_first(0, 0)
            pe.wait_ge(mat_lo_set, 6)
            turn_mat(4)
            pe.wait_ge(h0_t_saved, 2)
            turn_mat(5)
            run_slots(pe, slot)
            close_cand(LAST)
            pe.wait_ge(z_done, count(LAST, KC - 1))
            turn_state(LAST, STREAMS - 1, z_ps)


_INS = ["x", "adj", "L0_gnn_w3_w", "L0_gnn_w3_b", "L0_gnn_u3_w", "L0_gnn_u3_b", "L0_gnn_w4_w", "L0_gnn_w4_b",
        "L0_gnn_w5_w", "L0_gnn_w5_b", "L0_gnn_u5_w", "L0_gnn_u5_b"]


def kernel(**inputs):
    import numpy as _np
    import concourse.bacc as _bacc
    from concourse import mybir as _mybir
    from concourse.bass_utils import run_bass_kernel_spmd as _run

    nc = _bacc.Bacc("TRN2", target_bir_lowering=False, num_devices=1)
    arrays, args = {}, []
    for name in _INS:
        a = _np.ascontiguousarray(inputs[name])
        arrays[f"in_{name}_dram"] = a
        args.append(nc.dram_tensor(f"in_{name}_dram", a.shape, _mybir.dt.from_np(a.dtype), kind="ExternalInput").ap())
    out = nc.dram_tensor("out_0_dram", inputs["x"].shape, _mybir.dt.float32, kind="ExternalOutput").ap()
    gated_graph_network(nc, *args, out)
    r = _run(nc, [arrays], core_ids=[0])
    return r.results[0]["out_0_dram"]
```
